# Optimizing a Trainium2 kernel written in Bass

```python
import numpy as np
import jax
import jax.numpy as jnp

def _softmax(x, axis=-1):
    return jax.nn.softmax(x, axis=axis)
def _gelu(x):
    return jax.nn.gelu(x, approximate=True)
def _silu(x):
    return jax.nn.silu(x)
def _sigmoid(x):
    return jax.nn.sigmoid(x)
def _layernorm(x, axis=-1, eps=1e-5):
    m = jnp.mean(x, axis=axis, keepdims=True)
    v = jnp.var(x, axis=axis, keepdims=True)
    return (x - m) / jnp.sqrt(v + eps)
def _scatter_add(tgt, idx, src, axis=0):
    return tgt.at[idx].add(src)
def _segment_sum(src, seg, n):
    return jax.ops.segment_sum(src, seg, n)

kernel_name = 'mk_conv_preact_d4_conv_nhwc1024_ceb4d6'

def setup_inputs(seed: int = 0):
    np.random.seed(seed)
    _w = jnp.asarray
    def _rec_inputs():
        import jax
        import jax.numpy as jnp
        _gk = jax.random.key(seed)
        x = 7.22e-05 + 1 * jax.random.normal(jax.random.fold_in(_gk, 1), (64, 16, 8, 1024), jnp.float32)
        return x
    x = _rec_inputs()
    def _L0_conv_setup():
        import jax, jax.numpy as jnp
        import numpy as np
        B, C, N, D = (64, 16, 8, 1024)
        key = jax.random.key(seed)
        k1, k2, k3 = jax.random.split(key, 3)
        coeffs = jax.random.normal(k1, (B, C, N, D), dtype=jnp.float32)
        bound = 1.0 / np.sqrt(D)
        W = jax.random.uniform(k2, (D, D), dtype=jnp.float32, minval=-bound, maxval=bound)
        b = jax.random.uniform(k3, (D,), dtype=jnp.float32, minval=-bound, maxval=bound)
        threshold = jnp.float32(0.1)
        return {'coeffs': coeffs, 'W': W, 'b': b, 'threshold': threshold}
    _L0_conv_all = _L0_conv_setup()
    _L0_conv_in = {k: v for k, v in _L0_conv_all.items() if k in ('W', 'b', 'threshold', )}
    del _L0_conv_all

    def _L1_conv_setup():
        import jax, jax.numpy as jnp
        import numpy as np
        B, C, N, D = (64, 16, 8, 1024)
        key = jax.random.key(seed)
        k1, k2, k3 = jax.random.split(key, 3)
        coeffs = jax.random.normal(k1, (B, C, N, D), dtype=jnp.float32)
        bound = 1.0 / np.sqrt(D)
        W = jax.random.uniform(k2, (D, D), dtype=jnp.float32, minval=-bound, maxval=bound)
        b = jax.random.uniform(k3, (D,), dtype=jnp.float32, minval=-bound, maxval=bound)
        threshold = jnp.float32(0.1)
        return {'coeffs': coeffs, 'W': W, 'b': b, 'threshold': threshold}
    _L1_conv_all = _L1_conv_setup()
    _L1_conv_in = {k: v for k, v in _L1_conv_all.items() if k in ('W', 'b', 'threshold', )}
    del _L1_conv_all

    def _L2_conv_setup():
        import jax, jax.numpy as jnp
        import numpy as np
        B, C, N, D = (64, 16, 8, 1024)
        key = jax.random.key(seed)
        k1, k2, k3 = jax.random.split(key, 3)
        coeffs = jax.random.normal(k1, (B, C, N, D), dtype=jnp.float32)
        bound = 1.0 / np.sqrt(D)
        W = jax.random.uniform(k2, (D, D), dtype=jnp.float32, minval=-bound, maxval=bound)
        b = jax.random.uniform(k3, (D,), dtype=jnp.float32, minval=-bound, maxval=bound)
        threshold = jnp.float32(0.1)
        return {'coeffs': coeffs, 'W': W, 'b': b, 'threshold': threshold}
    _L2_conv_all = _L2_conv_setup()
    _L2_conv_in = {k: v for k, v in _L2_conv_all.items() if k in ('W', 'b', 'threshold', )}
    del _L2_conv_all

    def _L3_conv_setup():
        import jax, jax.numpy as jnp
        import numpy as np
        B, C, N, D = (64, 16, 8, 1024)
        key = jax.random.key(seed)
        k1, k2, k3 = jax.random.split(key, 3)
        coeffs = jax.random.normal(k1, (B, C, N, D), dtype=jnp.float32)
        bound = 1.0 / np.sqrt(D)
        W = jax.random.uniform(k2, (D, D), dtype=jnp.float32, minval=-bound, maxval=bound)
        b = jax.random.uniform(k3, (D,), dtype=jnp.float32, minval=-bound, maxval=bound)
        threshold = jnp.float32(0.1)
        return {'coeffs': coeffs, 'W': W, 'b': b, 'threshold': threshold}
    _L3_conv_all = _L3_conv_setup()
    _L3_conv_in = {k: v for k, v in _L3_conv_all.items() if k in ('W', 'b', 'threshold', )}
    del _L3_conv_all

    return {
        "x": x,
        "L0_conv_W": _L0_conv_in["W"],
        "L0_conv_b": _L0_conv_in["b"],
        "L0_conv_threshold": _L0_conv_in["threshold"],
        "L1_conv_W": _L1_conv_in["W"],
        "L1_conv_b": _L1_conv_in["b"],
        "L1_conv_threshold": _L1_conv_in["threshold"],
        "L2_conv_W": _L2_conv_in["W"],
        "L2_conv_b": _L2_conv_in["b"],
        "L2_conv_threshold": _L2_conv_in["threshold"],
        "L3_conv_W": _L3_conv_in["W"],
        "L3_conv_b": _L3_conv_in["b"],
        "L3_conv_threshold": _L3_conv_in["threshold"],
    }

def reference(x, L0_conv_W, L0_conv_b, L0_conv_threshold, L1_conv_W, L1_conv_b, L1_conv_threshold, L2_conv_W, L2_conv_b, L2_conv_threshold, L3_conv_W, L3_conv_b, L3_conv_threshold):
    import jax
    import jax.numpy as jnp
    def _L0_conv_ref(coeffs, W, b, threshold):
        import jax, jax.numpy as jnp
        import numpy as np
        B, C, N, D = (64, 16, 8, 1024)
        gate = jax.nn.sigmoid(jnp.einsum('bcnd,ed->bcne', coeffs, W) + b)
        gated = coeffs * gate
        return jnp.where(jnp.abs(gated) < threshold, jnp.float32(0.0), gated)

    def _L1_conv_ref(coeffs, W, b, threshold):
        import jax, jax.numpy as jnp
        import numpy as np
        B, C, N, D = (64, 16, 8, 1024)
        gate = jax.nn.sigmoid(jnp.einsum('bcnd,ed->bcne', coeffs, W) + b)
        gated = coeffs * gate
        return jnp.where(jnp.abs(gated) < threshold, jnp.float32(0.0), gated)

    def _L2_conv_ref(coeffs, W, b, threshold):
        import jax, jax.numpy as jnp
        import numpy as np
        B, C, N, D = (64, 16, 8, 1024)
        gate = jax.nn.sigmoid(jnp.einsum('bcnd,ed->bcne', coeffs, W) + b)
        gated = coeffs * gate
        return jnp.where(jnp.abs(gated) < threshold, jnp.float32(0.0), gated)

    def _L3_conv_ref(coeffs, W, b, threshold):
        import jax, jax.numpy as jnp
        import numpy as np
        B, C, N, D = (64, 16, 8, 1024)
        gate = jax.nn.sigmoid(jnp.einsum('bcnd,ed->bcne', coeffs, W) + b)
        gated = coeffs * gate
        return jnp.where(jnp.abs(gated) < threshold, jnp.float32(0.0), gated)

    def _gn(v, G=32, eps=1e-5):
        B_, H_, W_, C_ = v.shape
        g = v.reshape(B_, H_, W_, G, C_ // G)
        m = jnp.mean(g, axis=(1, 2, 4), keepdims=True)
        s = jnp.var(g, axis=(1, 2, 4), keepdims=True)
        return ((g - m) / jnp.sqrt(s + eps)).reshape(v.shape)

    def _ln_c(v, eps=1e-6):
        m = jnp.mean(v, axis=-1, keepdims=True)
        s = jnp.var(v, axis=-1, keepdims=True)
        return (v - m) / jnp.sqrt(s + eps)

    def _ln_t(v, eps=1e-5):
        m = jnp.mean(v, axis=-1, keepdims=True)
        s = jnp.var(v, axis=-1, keepdims=True)
        return (v - m) / jnp.sqrt(s + eps)

    def _to_tokens(v):
        B_, H_, W_, C_ = v.shape
        return v.reshape(B_, H_ * W_, C_)
    def _from_tokens(t, like):
        return t.reshape(like.shape)

    x = x + _L0_conv_ref(_gn(x), L0_conv_W, L0_conv_b, L0_conv_threshold)
    x = x + _L1_conv_ref(_gn(x), L1_conv_W, L1_conv_b, L1_conv_threshold)
    x = x + _L2_conv_ref(_gn(x), L2_conv_W, L2_conv_b, L2_conv_threshold)
    x = x + _L3_conv_ref(_gn(x), L3_conv_W, L3_conv_b, L3_conv_threshold)
    return x


_drawn_inputs = setup_inputs


def setup_inputs(seed=0):
    import zlib

    import numpy as np

    out = dict(_drawn_inputs(seed))
    spreads = {}
    factors = {'L0_conv_b': 8.0, 'L1_conv_b': 26.46, 'L2_conv_b': 33.386, 'L3_conv_b': 40.787}
    for name, (base, spread) in spreads.items():
        noise = np.random.default_rng([zlib.crc32(name.encode()), seed]).standard_normal(out[name].shape)
        drawn = base * np.exp(spread * noise) if base else spread * noise
        out[name] = jnp.asarray(drawn.astype(out[name].dtype))
    for name, factor in factors.items():
        out[name] = (out[name] * factor).astype(out[name].dtype)
    return out
```

```python
from contextlib import ExitStack

import concourse.bass as bass
from concourse import mybir

P = 128
F32 = mybir.dt.float32
F16 = mybir.dt.float16
U32 = mybir.dt.uint32
ALU = mybir.AluOpType
ACT = mybir.ActivationFunctionType

LAYERS = 4
SAMPLES = 4
N_IN_SAMPLE = 128
ROWS = SAMPLES * N_IN_SAMPLE
EPS = 1e-5
X_SCALE = 256.0
W_SUM_LIMIT = 16384.0
W_SUM_FLOOR = 1e-30
GROUP = 3
TURN = 32


def build(nc, x_dram, w_dram, b_dram, thr_dram, out_dram):
    blocks, chunks = x_dram.shape[0], x_dram.shape[1]
    tiles = chunks
    steps_per_block = LAYERS * tiles
    piece = chunks * P

    with ExitStack() as ctx:
        def sb(name, shape, dt):
            return ctx.enter_context(nc.sbuf_tensor(name, shape, dt))

        def sem(name):
            return ctx.enter_context(nc.semaphore(name))

        w_hi = sb("w_hi", [P, LAYERS, tiles, piece], F16)
        w_lo = sb("w_lo", [P, LAYERS, tiles, piece], F16)
        resid = sb("resid", [P, chunks, ROWS], F32)
        normed = sb("normed", [P, chunks, ROWS], F32)
        n_hi = sb("n_hi", [P, 2, chunks, ROWS], F16)
        n_lo = sb("n_lo", [P, 2, chunks, ROWS], F16)
        gated = sb("gated", [P, 2, ROWS], F32)
        stage = sb("stage", [P, 4, ROWS], F32)
        stats = sb("stats", [P, 3, TURN], F32)
        stats_turned = sb("stats_turned", [P, 3, TURN], F32)
        group_stats = sb("group_stats", [P, 2, 2], F32)
        coef_turned = sb("coef_turned", [P, 2, 2], F32)
        coef = sb("coef", [P, 2, 2, TURN], F32)
        minus_half = sb("minus_half", [P, 1], F32)
        eps = sb("eps", [P, 1], F32)
        bias = sb("bias", [P, LAYERS, tiles], F32)
        threshold = sb("threshold", [P, LAYERS], F32)
        w_sum = sb("w_sum", [P, LAYERS, tiles], F32)
        w_max = sb("w_max", [P, LAYERS, tiles], F32)
        w_inv = sb("w_inv", [P, LAYERS, tiles], F32)
        w_scale = sb("w_scale", [P, LAYERS, tiles], F32)
        w_unscale = sb("w_unscale", [P, LAYERS, tiles], F32)
        z_scale = sb("z_scale", [P, LAYERS, tiles], F32)

        banks = ctx.enter_context(nc.psum_tensor("banks", [P, tiles, ROWS], F32))

        products = sem("products")
        gates = sem("gates")
        gated_ready = sem("gated_ready")
        magnitudes = sem("magnitudes")
        kept = sem("kept")
        summed = sem("summed")
        stats_ready = sem("stats_ready")
        turned = sem("turned")
        aggregated = sem("aggregated")
        inv_std = sem("inv_std")
        coef_ready = sem("coef_ready")
        spread = sem("spread")
        normed_ready = sem("normed_ready")
        hi_ready = sem("hi_ready")
        lo_ready = sem("lo_ready")
        var_eps = sem("var_eps")
        x_loaded = [sem(f"x_loaded{k}") for k in range(chunks)]
        stored = [sem(f"stored{j}") for j in range(4)]
        w_loaded = [sem(f"w_loaded{j}") for j in range(2)]
        w_summed = sem("w_summed")
        w_max_ready = sem("w_max_ready")
        w_limited = sem("w_limited")
        w_inverted = sem("w_inverted")
        w_scaled = sem("w_scaled")
        w_hi_ready = sem("w_hi_ready")
        w_ready = sem("w_ready")
        w_unscaled = sem("w_unscaled")
        z_scales = sem("z_scales")
        constants = sem("constants")
        params = sem("params")

        def stage_piece(q):
            return stage[:, 2 * (q % 2):2 * (q % 2) + 2, :].rearrange("p a n -> p (a n)")

        def of_sample(ap, s):
            return ap.rearrange("p (h r q) -> p h r q", h=2, q=2)[:, s // 2, :, s % 2]

        def first_tile(blk, layer):
            return blk * steps_per_block + layer * tiles

        block = ctx.enter_context(nc.Block())

        @block.sync
        def _(sp):
            def load_x(blk, k):
                sp.dma_start(resid[:, k, :], x_dram[blk, k]).then_inc(x_loaded[k], 16)

            def load_w(q):
                if q >= 2:
                    sp.wait_ge(w_ready, q - 1)
                sp.dma_start(stage_piece(q), w_dram[q // tiles, q % tiles]).then_inc(w_loaded[q % 2], 16)

            def turn_over(blk, more):
                for k in range(chunks):
                    sp.wait_ge(summed, first_tile(blk, LAYERS - 1) + k + 1)
                    if more:
                        load_x(blk + 1, k)
                    sp.dma_start(out_dram[blk, k], stage[:, k % 4, :]).then_inc(stored[k % 4], 16)

            load_w(0)
            load_w(1)
            load_x(0, 0)
            load_x(0, 1)
            sp.dma_start(bias[:], b_dram).then_inc(params, 16)
            sp.dma_start(threshold[:], thr_dram).then_inc(params, 16)
            for k in range(2, chunks):
                load_x(0, k)
            for q in range(2, LAYERS * tiles):
                load_w(q)
            turn_over(0, True)
            with sp.Fori(1, blocks - 1) as blk:
                turn_over(blk, True)
            turn_over(blocks - 1, False)
            for j in range(4):
                sp.wait_ge(stored[j], 16 * blocks * chunks // 4)

        @block.tensor
        def _(pe):
            def wait_w(layer, e, first):
                if first:
                    pe.wait_ge(w_ready, layer * tiles + e + 1)

            def add_chunk(layer, e, k):
                for w, n in ((w_hi, n_hi), (w_hi, n_lo), (w_lo, n_hi)):
                    last = nc.tensor.matmul(
                        banks[:, e, :], w[:, layer, e, k * P:(k + 1) * P], n[:, layer % 2, k, :],
                        start=(k == 0 and w is w_hi and n is n_hi), stop=(k == chunks - 1 and w is w_lo))
                if k == chunks - 1:
                    last.then_inc(products, 1)

            def layer_products(blk, layer, first):
                base = first_tile(blk, layer)
                for k in range(chunks):
                    pe.wait_ge(lo_ready, base + k + 1)
                    for e in range(GROUP):
                        if k == 0:
                            wait_w(layer, e, first)
                            if not (first and layer == 0):
                                pe.wait_ge(kept, base - tiles + e + 1)
                        add_chunk(layer, e, k)
                for e in range(GROUP, tiles):
                    wait_w(layer, e, first)
                    if not (first and layer == 0):
                        pe.wait_ge(kept, base - tiles + e + 1)
                    for k in range(chunks):
                        add_chunk(layer, e, k)

            for layer in range(LAYERS):
                layer_products(0, layer, True)
            with pe.Fori(1, blocks) as blk:
                for layer in range(LAYERS):
                    layer_products(blk, layer, False)

        @block.scalar
        def _(act):
            def sum_piece(q):
                layer, e = divmod(q, tiles)
                act.wait_ge(w_loaded[q % 2], 16 * (q // 2 + 1))
                nc.scalar.activation(w_hi[:, layer, e, :], stage_piece(q), ACT.Abs,
                                     accum_out=w_sum[:, layer, e:e + 1]).then_inc(w_summed, 1)

            def split_piece(q):
                layer, e = divmod(q, tiles)
                act.wait_ge(w_scaled, q + 1)
                nc.scalar.activation(w_hi[:, layer, e, :], stage_piece(q), ACT.Copy,
                                     scale=w_scale[:, layer, e:e + 1]).then_inc(w_hi_ready, 1)

            def gate(blk, layer, e):
                t = first_tile(blk, layer) + e
                act.wait_ge(products, t + 1)
                nc.scalar.activation(banks[:, e, :], banks[:, e, :], ACT.Sigmoid,
                                     bias=bias[:, layer, e:e + 1],
                                     scale=z_scale[:, layer, e:e + 1]).then_inc(gates, 1)

            def magnitude(blk, layer, e):
                t = first_tile(blk, layer) + e
                act.wait_ge(gated_ready, t + 1)
                nc.scalar.activation(banks[:, e, :], gated[:, e % 2, :], ACT.Abs).then_inc(magnitudes, 1)

            def normalise(n, k):
                act.wait_ge(spread, n + 1)
                for s in range(SAMPLES):
                    last = nc.scalar.activation(
                        of_sample(normed[:, k, :], s), of_sample(resid[:, k, :], s), ACT.Identity,
                        scale=coef[:, k % 2, 0, s:s + 1], bias=coef[:, k % 2, 1, s:s + 1])
                last.then_inc(normed_ready, 1)

            def high_part(n, k, half):
                act.wait_ge(normed_ready, n + 1)
                nc.scalar.activation(n_hi[:, half, k, :], normed[:, k, :], ACT.Copy,
                                     scale=X_SCALE).then_inc(hi_ready, 1)

            def finish(blk, layer, first=False, more=True):
                last_layer = layer == LAYERS - 1
                to_norm = first_tile(blk, layer) + tiles
                if first:
                    act.wait_ge(z_scales, layer + 1)
                for s in range(tiles + 2):
                    if s < tiles:
                        gate(blk, layer, s)
                    if s >= 2 and more:
                        normalise(to_norm + s - 2, s - 2)
                    if s < tiles:
                        magnitude(blk, layer, s)
                    if s >= 2 and more:
                        high_part(to_norm + s - 2, s - 2, (layer + 1) % 2)
                    if first and not last_layer:
                        if s < tiles:
                            sum_piece((layer + 1) * tiles + s)
                        if 1 <= s <= tiles:
                            split_piece((layer + 1) * tiles + s - 1)

            act.wait_ge(params, 32)
            for k in range(chunks):
                sum_piece(k)
                normalise(k, k)
                high_part(k, k, 0)
                split_piece(k)
            for layer in range(LAYERS):
                finish(0, layer, first=True)
            with act.Fori(1, blocks - 1) as blk:
                for layer in range(LAYERS):
                    finish(blk, layer)
            for layer in range(LAYERS):
                finish(blocks - 1, layer, more=layer < LAYERS - 1)

        @block.vector
        def _(dve):
            def gating(blk, layer, e):
                t = first_tile(blk, layer) + e
                dve.wait_ge(gates, t + 1)
                nc.vector.tensor_tensor(gated[:, e % 2, :], normed[:, e, :], banks[:, e, :],
                                        ALU.mult).then_inc(gated_ready, 1)

            def keep(blk, layer, e):
                t = first_tile(blk, layer) + e
                dve.wait_ge(magnitudes, t + 1)
                nc.vector.scalar_tensor_tensor(
                    out=gated[:, e % 2, :], in0=banks[:, e, :], scalar=threshold[:, layer:layer + 1],
                    in1=gated[:, e % 2, :], op0=ALU.is_ge, op1=ALU.mult).then_inc(kept, 1)

            def statistics(n, k):
                for h in range(2):
                    half = resid[:, k, h * 2 * N_IN_SAMPLE:(h + 1) * 2 * N_IN_SAMPLE]
                    last = nc.vector.bn_stats(
                        stats[:, :, 2 * h:2 * h + 2].rearrange("p v s -> p s v"), half)
                last.then_inc(stats_ready, 1)
                dve.wait_ge(stats_ready, n + 1)
                nc.vector.transpose(stats_turned[:].rearrange("p v c -> p (v c)"),
                                    stats[:].rearrange("p v c -> p (v c)")).then_inc(turned, 1)
                dve.wait_ge(constants, 3)
                dve.wait_ge(turned, n + 1)
                nc.vector.bn_aggr(group_stats[:, k % 2, :],
                                  stats_turned[:].rearrange("p v c -> p c v")).then_inc(aggregated, 1)

            def spread_coef(n, k):
                dve.wait_ge(coef_ready, n + 1)
                nc.vector.transpose(coef[:, k % 2, :, :],
                                    coef_turned[:, k % 2, :].unsqueeze(2).to_broadcast([P, 2, TURN]))\
                    .then_inc(spread, 1)

            def low_part(n, k, half):
                dve.wait_ge(hi_ready, n + 1)
                nc.vector.scalar_tensor_tensor(
                    out=n_lo[:, half, k, :], in0=normed[:, k, :], scalar=X_SCALE,
                    in1=n_hi[:, half, k, :], op0=ALU.mult, op1=ALU.subtract).then_inc(lo_ready, 1)

            def scale_piece(q):
                layer, e = divmod(q, tiles)
                col = slice(e, e + 1)
                dve.wait_ge(w_limited, q + 1)
                nc.vector.reciprocal(w_inv[:, layer, col], w_max[:, layer, col]).then_inc(w_inverted, 1)
                dve.wait_ge(w_inverted, q + 1)
                nc.vector.tensor_scalar(w_scale[:, layer, col].bitcast(U32), w_inv[:, layer, col].bitcast(U32),
                                        0x7F800000, None, ALU.bitwise_and).then_inc(w_scaled, 1)

            def low_piece(q):
                layer, e = divmod(q, tiles)
                dve.wait_ge(w_hi_ready, q + 1)
                nc.vector.scalar_tensor_tensor(
                    out=w_lo[:, layer, e, :], in0=stage_piece(q), scalar=w_scale[:, layer, e:e + 1],
                    in1=w_hi[:, layer, e, :], op0=ALU.mult, op1=ALU.subtract).then_inc(w_ready, 1)

            def layer_scales(layer):
                nc.vector.reciprocal(w_unscale[:, layer, :], w_scale[:, layer, :]).then_inc(w_unscaled, 1)
                dve.wait_ge(w_unscaled, layer + 1)
                nc.vector.tensor_scalar(z_scale[:, layer, :], w_unscale[:, layer, :], 1.0 / X_SCALE, None,
                                        ALU.mult).then_inc(z_scales, 1)

            def finish(blk, layer, first=False, more=True):
                last_layer = layer == LAYERS - 1
                to_norm = first_tile(blk, layer) + tiles
                for s in range(tiles + 2):
                    if s >= 2 and more:
                        spread_coef(to_norm + s - 2, s - 2)
                    if 2 <= s < tiles and not more:
                        dve.wait_ge(summed, first_tile(blk, layer) + s - 1)
                    if s < tiles:
                        gating(blk, layer, s)
                    if 1 <= s <= tiles and more:
                        if last_layer:
                            dve.wait_ge(x_loaded[s - 1], 16 * (blk + 2))
                        else:
                            dve.wait_ge(summed, first_tile(blk, layer) + s)
                        statistics(to_norm + s - 1, s - 1)
                    if s < tiles:
                        keep(blk, layer, s)
                    if s >= 2 and more:
                        low_part(to_norm + s - 2, s - 2, (layer + 1) % 2)
                    if first and not last_layer:
                        if s < tiles:
                            scale_piece((layer + 1) * tiles + s)
                        if 1 <= s <= tiles:
                            low_piece((layer + 1) * tiles + s - 1)
                        if s == tiles:
                            layer_scales(layer + 1)

            nc.vector.memset(minus_half[:], -0.5).then_inc(constants, 1)
            nc.vector.memset(eps[:], EPS).then_inc(constants, 1)
            nc.vector.memset(stats[:], 1.0).then_inc(constants, 1)
            dve.wait_ge(constants, 3)
            dve.wait_ge(params, 32)
            for k in range(chunks + 1):
                if k < chunks:
                    dve.wait_ge(x_loaded[k], 16)
                    statistics(k, k)
                    scale_piece(k)
                    spread_coef(k, k)
                    low_part(k, k, 0)
                    low_piece(k)
            layer_scales(0)
            for layer in range(LAYERS):
                finish(0, layer, first=True)
            with dve.Fori(1, blocks - 1) as blk:
                for layer in range(LAYERS):
                    finish(blk, layer)
            for layer in range(LAYERS):
                finish(blocks - 1, layer, more=layer < LAYERS - 1)

        @block.gpsimd
        def _(pool):
            def coefficients(n, k):
                ring = k % 2
                mean, var = group_stats[:, ring, 0:1], group_stats[:, ring, 1:2]
                std_inv, shift = coef_turned[:, ring, 0:1], coef_turned[:, ring, 1:2]
                pool.wait_ge(aggregated, n + 1)
                nc.gpsimd.tensor_tensor(var, var, eps[:], ALU.add).then_inc(var_eps, 1)
                pool.wait_ge(var_eps, n + 1)
                nc.gpsimd.tensor_tensor(std_inv, var, minus_half[:], ALU.pow).then_inc(inv_std, 1)
                pool.wait_ge(constants, 3)
                pool.wait_ge(inv_std, n + 1)
                nc.gpsimd.tensor_scalar(shift, mean, std_inv, -1.0, ALU.mult, ALU.mult).then_inc(coef_ready, 1)

            def add(blk, layer, e, first):
                t = first_tile(blk, layer) + e
                pool.wait_ge(kept, t + 1)
                if layer < LAYERS - 1:
                    out = resid[:, e, :]
                else:
                    out = stage[:, e % 4, :]
                    if not first:
                        pool.wait_ge(stored[e % 4], 32 * blk + 16 * (e // 4))
                    elif e >= 4:
                        pool.wait_ge(stored[e % 4], 16)
                nc.gpsimd.tensor_tensor(out, resid[:, e, :], gated[:, e % 2, :], ALU.add).then_inc(summed, 1)

            def limit_piece(q):
                layer, e = divmod(q, tiles)
                col = slice(e, e + 1)
                pool.wait_ge(w_summed, q + 1)
                nc.gpsimd.partition_all_reduce(w_max[:, layer, col], w_sum[:, layer, col], P,
                                               bass.bass_isa.ReduceOp.max).then_inc(w_max_ready, 1)
                pool.wait_ge(w_max_ready, q + 1)
                nc.gpsimd.tensor_scalar(w_max[:, layer, col], w_max[:, layer, col], 1.0 / W_SUM_LIMIT,
                                        W_SUM_FLOOR, ALU.mult, ALU.max).then_inc(w_limited, 1)

            def finish(blk, layer, first=False, more=True):
                to_norm = first_tile(blk, layer) + tiles
                for s in range(tiles + 1):
                    if s >= 1 and more:
                        if s < tiles:
                            coefficients(to_norm + s - 1, s - 1)
                    if s < tiles:
                        add(blk, layer, s, first)
                    if s == tiles and more:
                        coefficients(to_norm + s - 1, s - 1)
                    if first and layer < LAYERS - 1 and s < tiles:
                        limit_piece((layer + 1) * tiles + s)

            pool.wait_ge(constants, 3)
            for k in range(chunks):
                limit_piece(k)
                coefficients(k, k)
            for layer in range(LAYERS):
                finish(0, layer, first=True)
            with pool.Fori(1, blocks - 1) as blk:
                for layer in range(LAYERS):
                    finish(blk, layer)
            for layer in range(LAYERS):
                finish(blocks - 1, layer, more=layer < LAYERS - 1)


def kernel(**inputs):
    import numpy as np
    import concourse.bacc as bacc
    from concourse.bass_utils import run_bass_kernel_spmd

    x = np.asarray(inputs["x"])
    d = x.shape[-1]
    chunks, blocks = d // P, x.shape[0] // SAMPLES
    xt = x.reshape(blocks, 2, 2, N_IN_SAMPLE, chunks, P).transpose(0, 4, 5, 1, 3, 2)
    w = [np.asarray(inputs[f"L{i}_conv_W"]).reshape(chunks, P, chunks, P).transpose(0, 3, 2, 1)
         for i in range(LAYERS)]
    b = [np.asarray(inputs[f"L{i}_conv_b"]).reshape(chunks, P).T for i in range(LAYERS)]
    thr = [np.broadcast_to(np.asarray(inputs[f"L{i}_conv_threshold"]).reshape(1, 1), (P, 1))
           for i in range(LAYERS)]
    arrays = {
        "x_t": np.ascontiguousarray(xt).reshape(blocks, chunks, P, ROWS),
        "w_t": np.ascontiguousarray(np.stack(w)).reshape(LAYERS, chunks, P, chunks * P),
        "b_t": np.ascontiguousarray(np.stack(b, axis=1)),
        "thr_t": np.ascontiguousarray(np.concatenate(thr, axis=1)),
    }
    nc = bacc.Bacc("TRN2", target_bir_lowering=False, num_devices=1)
    args = [nc.dram_tensor(name, a.shape, mybir.dt.from_np(a.dtype), kind="ExternalInput").ap()
            for name, a in arrays.items()]
    out = nc.dram_tensor("out_t", (blocks, chunks, P, ROWS), F32, kind="ExternalOutput").ap()
    build(nc, *args, out)
    r = run_bass_kernel_spmd(nc, [arrays], core_ids=[0])
    got = r.results[0]["out_t"].reshape(blocks, chunks, P, 2, N_IN_SAMPLE, 2)
    return np.ascontiguousarray(got.transpose(0, 3, 5, 4, 1, 2)).reshape(x.shape)
```

```python
from contextlib import ExitStack

import concourse.bass as bass
from concourse import mybir

P = 128
F32 = mybir.dt.float32
F16 = mybir.dt.float16
U32 = mybir.dt.uint32
ALU = mybir.AluOpType
ACT = mybir.ActivationFunctionType

LAYERS = 4
SAMPLES = 4
N_IN_SAMPLE = 128
ROWS = SAMPLES * N_IN_SAMPLE
EPS = 1e-5
X_SCALE = 256.0
W_SUM_LIMIT = 16384.0
W_SUM_FLOOR = 1e-30
GROUP = 4
AHEAD = 5
TURN = 32


def build(nc, x_dram, w_dram, b_dram, thr_dram, out_dram):
    blocks, chunks = x_dram.shape[0], x_dram.shape[1]
    tiles = chunks
    steps_per_block = LAYERS * tiles
    pieces = LAYERS * tiles
    piece = chunks * P

    with ExitStack() as ctx:
        def sb(name, shape, dt):
            return ctx.enter_context(nc.sbuf_tensor(name, shape, dt))

        def sem(name):
            return ctx.enter_context(nc.semaphore(name))

        w_hi = sb("w_hi", [P, LAYERS, tiles, piece], F16)
        w_lo = sb("w_lo", [P, LAYERS, tiles, piece], F16)
        resid = sb("resid", [P, chunks, ROWS], F32)
        normed = sb("normed", [P, chunks, ROWS], F32)
        n_hi = sb("n_hi", [P, 2, chunks, ROWS], F16)
        n_lo = sb("n_lo", [P, 2, chunks, ROWS], F16)
        gated = sb("gated", [P, 2, ROWS], F32)
        stage = sb("stage", [P, 4, ROWS], F32)
        stats = sb("stats", [P, 3, TURN], F32)
        stats_turned = sb("stats_turned", [P, 3, TURN], F32)
        group_stats = sb("group_stats", [P, 2, 2], F32)
        coef_turned = sb("coef_turned", [P, 2, 2], F32)
        coef = sb("coef", [P, 2, 2, TURN], F32)
        minus_half = sb("minus_half", [P, 1], F32)
        eps = sb("eps", [P, 1], F32)
        bias = sb("bias", [P, LAYERS, tiles], F32)
        threshold = sb("threshold", [P, LAYERS], F32)
        w_sum = sb("w_sum", [P, LAYERS, tiles], F32)
        w_max = sb("w_max", [P, LAYERS, tiles], F32)
        w_inv = sb("w_inv", [P, LAYERS, tiles], F32)
        w_scale = sb("w_scale", [P, LAYERS, tiles], F32)
        w_unscale = sb("w_unscale", [P, LAYERS, tiles], F32)
        z_scale = sb("z_scale", [P, LAYERS, tiles], F32)

        banks = ctx.enter_context(nc.psum_tensor("banks", [P, tiles, ROWS], F32))

        products = sem("products")
        gates = sem("gates")
        gated_ready = sem("gated_ready")
        magnitudes = sem("magnitudes")
        kept = sem("kept")
        summed = sem("summed")
        stats_ready = sem("stats_ready")
        turned = sem("turned")
        aggregated = sem("aggregated")
        inv_std = sem("inv_std")
        coef_ready = sem("coef_ready")
        spread = sem("spread")
        normed_ready = sem("normed_ready")
        hi_ready = sem("hi_ready")
        lo_ready = sem("lo_ready")
        var_eps = sem("var_eps")
        x_loaded = [sem(f"x_loaded{k}") for k in range(chunks)]
        stored = [sem(f"stored{j}") for j in range(4)]
        w_loaded = [sem(f"w_loaded{j}") for j in range(10)]
        w_summed = sem("w_summed")
        w_max_ready = sem("w_max_ready")
        w_limited = sem("w_limited")
        w_inverted = sem("w_inverted")
        w_scaled = sem("w_scaled")
        w_hi_ready = sem("w_hi_ready")
        w_ready = sem("w_ready")
        w_unscaled = sem("w_unscaled")
        z_scales = sem("z_scales")
        constants = sem("constants")
        params = sem("params")

        landings = [part[:, LAYERS - 1, 2 * j:2 * j + 2, :].rearrange("p a n -> p (a n)").bitcast(F32)
                    for j in range(tiles // 2) for part in (w_hi, w_lo)]
        landings += [stage[:, 2 * j:2 * j + 2, :].rearrange("p a n -> p (a n)") for j in range(2)]
        last_landings = [4, 5, 6, 8, 9, 7, 8, 9]

        def landing(q):
            layer, e = divmod(q, tiles)
            return last_landings[e] if layer == LAYERS - 1 else q % len(landings)

        def before(q):
            return max((r for r in range(q) if landing(r) == landing(q)), default=None)

        def loads_until(q):
            return 16 * sum(landing(r) == landing(q) for r in range(q + 1))

        def stage_piece(q):
            return landings[landing(q)]

        def lag(layer):
            return 2 if layer == LAYERS - 1 else 1

        def of_sample(ap, s):
            return ap.rearrange("p (h r q) -> p h r q", h=2, q=2)[:, s // 2, :, s % 2]

        def first_tile(blk, layer):
            return blk * steps_per_block + layer * tiles

        block = ctx.enter_context(nc.Block())

        @block.sync
        def _(sp):
            def load_x(blk, k):
                sp.dma_start(resid[:, k, :], x_dram[blk, k]).then_inc(x_loaded[k], 16)

            def load_w(q):
                if before(q) is not None:
                    sp.wait_ge(w_ready, before(q) + 1)
                sp.dma_start(stage_piece(q), w_dram[q // tiles, q % tiles]).then_inc(w_loaded[landing(q)], 16)

            def turn_over(blk, more):
                for k in range(chunks):
                    sp.wait_ge(summed, first_tile(blk, LAYERS - 1) + k + 1)
                    if more:
                        load_x(blk + 1, k)
                    sp.dma_start(out_dram[blk, k], stage[:, k % 4, :]).then_inc(stored[k % 4], 16)

            for k in range(chunks):
                load_x(0, k)
                load_w(k)
                if k == GROUP:
                    sp.dma_start(bias[:], b_dram).then_inc(params, 16)
                    sp.dma_start(threshold[:], thr_dram).then_inc(params, 16)
            for q in range(tiles, pieces):
                load_w(q)
            turn_over(0, True)
            with sp.Fori(1, blocks - 1) as blk:
                turn_over(blk, True)
            turn_over(blocks - 1, False)
            for j in range(4):
                sp.wait_ge(stored[j], 16 * blocks * chunks // 4)

        @block.tensor
        def _(pe):
            def wait_w(layer, e, first):
                if first:
                    pe.wait_ge(w_ready, layer * tiles + e + 1)

            def add_chunk(layer, e, k):
                for w, n in ((w_hi, n_hi), (w_hi, n_lo), (w_lo, n_hi)):
                    last = nc.tensor.matmul(
                        banks[:, e, :], w[:, layer, e, k * P:(k + 1) * P], n[:, layer % 2, k, :],
                        start=(k == 0 and w is w_hi and n is n_hi), stop=(k == chunks - 1 and w is w_lo))
                if k == chunks - 1:
                    last.then_inc(products, 1)

            def layer_products(blk, layer, first):
                base = first_tile(blk, layer)
                for k in range(chunks):
                    pe.wait_ge(lo_ready, base + k + 1)
                    for e in range(GROUP):
                        if k == 0:
                            wait_w(layer, e, first)
                            if not (first and layer == 0):
                                pe.wait_ge(kept, base - tiles + e + 1)
                        add_chunk(layer, e, k)
                for e in range(GROUP, tiles):
                    wait_w(layer, e, first)
                    if not (first and layer == 0):
                        pe.wait_ge(kept, base - tiles + e + 1)
                    for k in range(chunks):
                        add_chunk(layer, e, k)

            for layer in range(LAYERS):
                layer_products(0, layer, True)
            with pe.Fori(1, blocks) as blk:
                for layer in range(LAYERS):
                    layer_products(blk, layer, False)

        @block.scalar
        def _(act):
            def sum_piece(q):
                layer, e = divmod(q, tiles)
                act.wait_ge(w_loaded[landing(q)], loads_until(q))
                nc.scalar.activation(w_hi[:, layer, e, :], stage_piece(q), ACT.Abs,
                                     accum_out=w_sum[:, layer, e:e + 1]).then_inc(w_summed, 1)

            def gate(blk, layer, e):
                t = first_tile(blk, layer) + e
                act.wait_ge(products, t + 1)
                nc.scalar.activation(banks[:, e, :], banks[:, e, :], ACT.Sigmoid,
                                     bias=bias[:, layer, e:e + 1],
                                     scale=z_scale[:, layer, e:e + 1]).then_inc(gates, 1)

            def magnitude(blk, layer, e):
                t = first_tile(blk, layer) + e
                act.wait_ge(gated_ready, t + 1)
                nc.scalar.activation(banks[:, e, :], gated[:, e % 2, :], ACT.Abs).then_inc(magnitudes, 1)

            def normalise(n, k):
                act.wait_ge(spread, n + 1)
                for s in range(SAMPLES):
                    last = nc.scalar.activation(
                        of_sample(normed[:, k, :], s), of_sample(resid[:, k, :], s), ACT.Identity,
                        scale=coef[:, k % 2, 0, s:s + 1], bias=coef[:, k % 2, 1, s:s + 1])
                last.then_inc(normed_ready, 1)

            def high_part(n, k, half):
                act.wait_ge(normed_ready, n + 1)
                nc.scalar.activation(n_hi[:, half, k, :], normed[:, k, :], ACT.Copy,
                                     scale=X_SCALE).then_inc(hi_ready, 1)

            def finish(blk, layer, first=False, more=True):
                to_norm = first_tile(blk, layer) + tiles
                piece0 = (layer + 1) * tiles + AHEAD
                if first:
                    act.wait_ge(z_scales, layer + 1)
                for s in range(tiles + lag(layer) + 1):
                    k = s - lag(layer) - 1
                    if s < tiles:
                        gate(blk, layer, s)
                    if k >= 0 and more:
                        normalise(to_norm + k, k)
                    if s < tiles:
                        magnitude(blk, layer, s)
                    if k >= 0 and more:
                        high_part(to_norm + k, k, (layer + 1) % 2)
                    if first and s < tiles and piece0 + s < pieces:
                        sum_piece(piece0 + s)

            for k in range(chunks):
                if k == 0:
                    sum_piece(0)
                sum_piece(k + 1)
                normalise(k, k)
                high_part(k, k, 0)
            for q in range(chunks + 1, chunks + AHEAD):
                sum_piece(q)
            act.wait_ge(params, 32)
            for layer in range(LAYERS):
                finish(0, layer, first=True)
            with act.Fori(1, blocks - 1) as blk:
                for layer in range(LAYERS):
                    finish(blk, layer)
            for layer in range(LAYERS):
                finish(blocks - 1, layer, more=layer < LAYERS - 1)

        @block.vector
        def _(dve):
            def gating(blk, layer, e):
                t = first_tile(blk, layer) + e
                dve.wait_ge(gates, t + 1)
                nc.vector.tensor_tensor(gated[:, e % 2, :], normed[:, e, :], banks[:, e, :],
                                        ALU.mult).then_inc(gated_ready, 1)

            def keep(blk, layer, e):
                t = first_tile(blk, layer) + e
                dve.wait_ge(magnitudes, t + 1)
                nc.vector.scalar_tensor_tensor(
                    out=gated[:, e % 2, :], in0=banks[:, e, :], scalar=threshold[:, layer:layer + 1],
                    in1=gated[:, e % 2, :], op0=ALU.is_ge, op1=ALU.mult).then_inc(kept, 1)

            def statistics(n, k):
                for h in range(2):
                    half = resid[:, k, h * 2 * N_IN_SAMPLE:(h + 1) * 2 * N_IN_SAMPLE]
                    last = nc.vector.bn_stats(
                        stats[:, :, 2 * h:2 * h + 2].rearrange("p v s -> p s v"), half)
                last.then_inc(stats_ready, 1)
                dve.wait_ge(stats_ready, n + 1)
                nc.vector.transpose(stats_turned[:].rearrange("p v c -> p (v c)"),
                                    stats[:].rearrange("p v c -> p (v c)")).then_inc(turned, 1)
                dve.wait_ge(constants, 3)
                dve.wait_ge(turned, n + 1)
                nc.vector.bn_aggr(group_stats[:, k % 2, :],
                                  stats_turned[:].rearrange("p v c -> p c v")).then_inc(aggregated, 1)

            def spread_coef(n, k):
                dve.wait_ge(coef_ready, n + 1)
                nc.vector.transpose(coef[:, k % 2, :, :],
                                    coef_turned[:, k % 2, :].unsqueeze(2).to_broadcast([P, 2, TURN]))\
                    .then_inc(spread, 1)

            def low_part(n, k, half):
                dve.wait_ge(hi_ready, n + 1)
                nc.vector.scalar_tensor_tensor(
                    out=n_lo[:, half, k, :], in0=normed[:, k, :], scalar=X_SCALE,
                    in1=n_hi[:, half, k, :], op0=ALU.mult, op1=ALU.subtract).then_inc(lo_ready, 1)

            def scale_piece(q):
                layer, e = divmod(q, tiles)
                col = slice(e, e + 1)
                dve.wait_ge(w_limited, q + 1)
                nc.vector.reciprocal(w_inv[:, layer, col], w_max[:, layer, col]).then_inc(w_inverted, 1)
                dve.wait_ge(w_inverted, q + 1)
                nc.vector.tensor_scalar(w_scale[:, layer, col].bitcast(U32), w_inv[:, layer, col].bitcast(U32),
                                        0x7F800000, None, ALU.bitwise_and).then_inc(w_scaled, 1)

            def low_piece(q):
                layer, e = divmod(q, tiles)
                dve.wait_ge(w_hi_ready, q + 1)
                nc.vector.scalar_tensor_tensor(
                    out=w_lo[:, layer, e, :], in0=stage_piece(q), scalar=w_scale[:, layer, e:e + 1],
                    in1=w_hi[:, layer, e, :], op0=ALU.mult, op1=ALU.subtract).then_inc(w_ready, 1)

            def layer_scales(layer):
                nc.vector.reciprocal(w_unscale[:, layer, :], w_scale[:, layer, :]).then_inc(w_unscaled, 1)
                dve.wait_ge(w_unscaled, layer + 1)
                nc.vector.tensor_scalar(z_scale[:, layer, :], w_unscale[:, layer, :], 1.0 / X_SCALE, None,
                                        ALU.mult).then_inc(z_scales, 1)

            def finish(blk, layer, first=False, more=True):
                last_layer = layer == LAYERS - 1
                to_norm = first_tile(blk, layer) + tiles
                piece0 = (layer + 1) * tiles + AHEAD
                for s in range(tiles + lag(layer) + 1):
                    c, k = s - lag(layer), s - lag(layer) - 1
                    if k >= 0 and more:
                        spread_coef(to_norm + k, k)
                    if 2 <= s < tiles and last_layer:
                        dve.wait_ge(summed, first_tile(blk, layer) + s - 1)
                    if s < tiles:
                        gating(blk, layer, s)
                    if 0 <= c < tiles and more:
                        if last_layer:
                            dve.wait_ge(x_loaded[c], 16 * (blk + 2))
                        else:
                            dve.wait_ge(summed, first_tile(blk, layer) + c + 1)
                        statistics(to_norm + c, c)
                    if s < tiles:
                        keep(blk, layer, s)
                    if first and 1 <= s <= tiles and piece0 + s - 1 < pieces:
                        scale_piece(piece0 + s - 1)
                    if k >= 0 and more:
                        low_part(to_norm + k, k, (layer + 1) % 2)
                    if first and 2 <= s <= tiles + 1 and piece0 + s - 2 < pieces:
                        low_piece(piece0 + s - 2)
                if first and not last_layer:
                    layer_scales(layer + 1)

            nc.vector.memset(minus_half[:], -0.5).then_inc(constants, 1)
            nc.vector.memset(eps[:], EPS).then_inc(constants, 1)
            nc.vector.memset(stats[:], 1.0).then_inc(constants, 1)
            dve.wait_ge(constants, 3)
            for k in range(-1, chunks + 1):
                if k + 1 < chunks:
                    dve.wait_ge(x_loaded[k + 1], 16)
                    statistics(k + 1, k + 1)
                if 0 <= k < chunks:
                    spread_coef(k, k)
                if k > 0:
                    low_part(k - 1, k - 1, 0)
                if 0 <= k < chunks:
                    scale_piece(k)
                if k > 0:
                    low_piece(k - 1)
            layer_scales(0)
            for q in range(chunks, chunks + AHEAD):
                scale_piece(q)
                if q > chunks:
                    low_piece(q - 1)
            low_piece(chunks + AHEAD - 1)
            dve.wait_ge(params, 32)
            for layer in range(LAYERS):
                finish(0, layer, first=True)
            with dve.Fori(1, blocks - 1) as blk:
                for layer in range(LAYERS):
                    finish(blk, layer)
            for layer in range(LAYERS):
                finish(blocks - 1, layer, more=layer < LAYERS - 1)

        @block.gpsimd
        def _(pool):
            def coefficients(n, k):
                ring = k % 2
                mean, var = group_stats[:, ring, 0:1], group_stats[:, ring, 1:2]
                std_inv, shift = coef_turned[:, ring, 0:1], coef_turned[:, ring, 1:2]
                pool.wait_ge(aggregated, n + 1)
                nc.gpsimd.tensor_tensor(var, var, eps[:], ALU.add).then_inc(var_eps, 1)
                pool.wait_ge(var_eps, n + 1)
                nc.gpsimd.tensor_tensor(std_inv, var, minus_half[:], ALU.pow).then_inc(inv_std, 1)
                pool.wait_ge(constants, 3)
                pool.wait_ge(inv_std, n + 1)
                nc.gpsimd.tensor_scalar(shift, mean, std_inv, -1.0, ALU.mult, ALU.mult).then_inc(coef_ready, 1)

            def add(blk, layer, e, first):
                t = first_tile(blk, layer) + e
                pool.wait_ge(kept, t + 1)
                if layer < LAYERS - 1:
                    out = resid[:, e, :]
                else:
                    out = stage[:, e % 4, :]
                    if not first:
                        pool.wait_ge(stored[e % 4], 32 * blk + 16 * (e // 4))
                    elif e >= 4:
                        pool.wait_ge(stored[e % 4], 16)
                nc.gpsimd.tensor_tensor(out, resid[:, e, :], gated[:, e % 2, :], ALU.add).then_inc(summed, 1)

            def limit_piece(q):
                layer, e = divmod(q, tiles)
                col = slice(e, e + 1)
                pool.wait_ge(w_summed, q + 1)
                nc.gpsimd.partition_all_reduce(w_max[:, layer, col], w_sum[:, layer, col], P,
                                               bass.bass_isa.ReduceOp.max).then_inc(w_max_ready, 1)
                pool.wait_ge(w_max_ready, q + 1)
                nc.gpsimd.tensor_scalar(w_max[:, layer, col], w_max[:, layer, col], 1.0 / W_SUM_LIMIT,
                                        W_SUM_FLOOR, ALU.mult, ALU.max).then_inc(w_limited, 1)

            def split_piece(q):
                layer, e = divmod(q, tiles)
                pool.wait_ge(w_scaled, q + 1)
                nc.gpsimd.tensor_scalar(w_hi[:, layer, e, :], stage_piece(q), w_scale[:, layer, e:e + 1], 1.0,
                                        ALU.mult, ALU.mult).then_inc(w_hi_ready, 1)

            def finish(blk, layer, first=False, more=True):
                to_norm = first_tile(blk, layer) + tiles
                piece0 = (layer + 1) * tiles + AHEAD
                for s in range(tiles + lag(layer)):
                    c = s - lag(layer)
                    if first and 1 <= s <= tiles and piece0 + s - 1 < pieces:
                        limit_piece(piece0 + s - 1)
                    if c >= 0 and more:
                        coefficients(to_norm + c, c)
                    if s < tiles:
                        add(blk, layer, s, first)
                    if first and 1 <= s <= tiles and piece0 + s - 1 < pieces:
                        split_piece(piece0 + s - 1)

            pool.wait_ge(constants, 3)
            for k in range(chunks):
                coefficients(k, k)
                limit_piece(k)
                split_piece(k)
            limit_piece(chunks)
            for q in range(chunks, chunks + AHEAD):
                if q + 1 < chunks + AHEAD:
                    limit_piece(q + 1)
                split_piece(q)
            for layer in range(LAYERS):
                finish(0, layer, first=True)
            with pool.Fori(1, blocks - 1) as blk:
                for layer in range(LAYERS):
                    finish(blk, layer)
            for layer in range(LAYERS):
                finish(blocks - 1, layer, more=layer < LAYERS - 1)


def kernel(**inputs):
    import numpy as np
    import concourse.bacc as bacc
    from concourse.bass_utils import run_bass_kernel_spmd

    x = np.asarray(inputs["x"])
    d = x.shape[-1]
    chunks, blocks = d // P, x.shape[0] // SAMPLES
    xt = x.reshape(blocks, 2, 2, N_IN_SAMPLE, chunks, P).transpose(0, 4, 5, 1, 3, 2)
    w = [np.asarray(inputs[f"L{i}_conv_W"]).reshape(chunks, P, chunks, P).transpose(0, 3, 2, 1)
         for i in range(LAYERS)]
    b = [np.asarray(inputs[f"L{i}_conv_b"]).reshape(chunks, P).T for i in range(LAYERS)]
    thr = [np.broadcast_to(np.asarray(inputs[f"L{i}_conv_threshold"]).reshape(1, 1), (P, 1))
           for i in range(LAYERS)]
    arrays = {
        "x_t": np.ascontiguousarray(xt).reshape(blocks, chunks, P, ROWS),
        "w_t": np.ascontiguousarray(np.stack(w)).reshape(LAYERS, chunks, P, chunks * P),
        "b_t": np.ascontiguousarray(np.stack(b, axis=1)),
        "thr_t": np.ascontiguousarray(np.concatenate(thr, axis=1)),
    }
    nc = bacc.Bacc("TRN2", target_bir_lowering=False, num_devices=1)
    args = [nc.dram_tensor(name, a.shape, mybir.dt.from_np(a.dtype), kind="ExternalInput").ap()
            for name, a in arrays.items()]
    out = nc.dram_tensor("out_t", (blocks, chunks, P, ROWS), F32, kind="ExternalOutput").ap()
    build(nc, *args, out)
    r = run_bass_kernel_spmd(nc, [arrays], core_ids=[0])
    got = r.results[0]["out_t"].reshape(blocks, chunks, P, 2, N_IN_SAMPLE, 2)
    return np.ascontiguousarray(got.transpose(0, 3, 5, 4, 1, 2)).reshape(x.shape)
```
